# Optimizing a Trainium2 kernel written in Bass

```python
import numpy as np
import jax
import jax.numpy as jnp

def _softmax(x, axis=-1):
    return jax.nn.softmax(x, axis=axis)

def _gelu(x):
    return jax.nn.gelu(x, approximate=True)

def _silu(x):
    return jax.nn.silu(x)

def _sigmoid(x):
    return jax.nn.sigmoid(x)

def _layernorm(x, axis=-1, eps=1e-05):
    m = jnp.mean(x, axis=axis, keepdims=True)
    v = jnp.var(x, axis=axis, keepdims=True)
    return (x - m) / jnp.sqrt(v + eps)

def _scatter_add(tgt, idx, src, axis=0):
    return tgt.at[idx].add(src)

def _segment_sum(src, seg, n):
    return jax.ops.segment_sum(src, seg, n)
kernel_name = 'mk_gps_d1_gnn_r8_081df0'

def setup_inputs(seed: int=0):
    np.random.seed(seed)
    _w = jnp.asarray

    def _rec_inputs():
        import jax
        import jax.numpy as jnp
        _gk = jax.random.key(seed)
        x = -0.0003713 + 1 * jax.random.normal(jax.random.fold_in(_gk, 1), (6250, 256), jnp.float32)
        src = jax.random.randint(jax.random.fold_in(_gk, 2), (200000,), 0, 6250, jnp.int32)
        dst = jax.random.randint(jax.random.fold_in(_gk, 3), (200000,), 0, 6250, jnp.int32)
        _o = jnp.argsort(dst, stable=True)
        src = src[_o]
        dst = dst[_o]
        return (x, src, dst)
    x, src, dst = _rec_inputs()

    def _L0_gnn_setup():
        import jax, jax.numpy as jnp
        import numpy as np
        N_NODES = 6250
        N_EDGES = 200000
        H_SIZE = 256
        HEADS = 8
        HEAD_DIM = H_SIZE // HEADS
        NEG_SLOPE = 0.2
        key = jax.random.key(seed)
        k_x, k_e, k_w, k_as, k_ad, k_b = jax.random.split(key, 6)
        x = jax.random.normal(k_x, (N_NODES, H_SIZE), dtype=jnp.float32)
        edge_index = jax.random.randint(k_e, (2, N_EDGES), 0, N_NODES, dtype=jnp.int64)
        scale = 1.0 / np.sqrt(H_SIZE)
        W = jax.random.normal(k_w, (H_SIZE, HEADS, HEAD_DIM), dtype=jnp.float32) * scale
        att_src = jax.random.normal(k_as, (HEADS, HEAD_DIM), dtype=jnp.float32) * scale
        att_dst = jax.random.normal(k_ad, (HEADS, HEAD_DIM), dtype=jnp.float32) * scale
        bias = jnp.zeros((H_SIZE,), dtype=jnp.float32)
        return {'x': x, 'edge_index': edge_index, 'W': W, 'att_src': att_src, 'att_dst': att_dst, 'bias': bias}
    _L0_gnn_all = _L0_gnn_setup()
    _L0_gnn_in = {k: v for k, v in _L0_gnn_all.items() if k in ('W', 'att_src', 'att_dst', 'bias')}
    del _L0_gnn_all

    def _L0_mix_setup():
        import jax, jax.numpy as jnp
        import numpy as np
        HEADS = 4
        DIM_HEAD = 32
        key = jax.random.key(seed)
        k1, k2, k3 = jax.random.split(key, 3)
        B, L, D = (16, 1024, 256)
        hidden = HEADS * DIM_HEAD
        x = jax.random.normal(k1, (B, L, D), dtype=jnp.float32)
        W_qkv = jax.random.normal(k2, (D, 3 * hidden), dtype=jnp.float32) * D ** (-0.5)
        W_out = jax.random.normal(k3, (hidden, D), dtype=jnp.float32) * hidden ** (-0.5)
        b_out = jnp.zeros((D,), dtype=jnp.float32)
        return {'x': x, 'W_qkv': W_qkv, 'W_out': W_out, 'b_out': b_out}
    _L0_mix_all = _L0_mix_setup()
    _L0_mix_in = {k: v for k, v in _L0_mix_all.items() if k in ('W_qkv', 'W_out', 'b_out')}
    del _L0_mix_all

    def _L0_ffn_setup():
        import jax, jax.numpy as jnp
        import numpy as np
        BN_EPS = 0.001

        def _bn(h, g, b, m, v):
            return g * (h - m) * jax.lax.rsqrt(v + BN_EPS) + b
        key = jax.random.key(seed)
        ks = jax.random.split(key, 8)
        B, F, Df = (256, 64, 256)
        E, H, D = (8, 256, 256)
        s1 = 1.0 / np.sqrt(Df)
        s2 = 1.0 / np.sqrt(H)
        return {'x': jax.random.normal(ks[0], (B, F, Df), jnp.float32), 'Wr': jax.random.normal(ks[1], (Df, E), jnp.float32) * s1, 'br': jnp.zeros((E,), jnp.float32), 'W1': jax.random.normal(ks[2], (E, Df, H), jnp.float32) * s1, 'b1': jnp.zeros((E, H), jnp.float32), 'g1': jnp.ones((E, H), jnp.float32), 'be1': jnp.zeros((E, H), jnp.float32), 'm1': jnp.zeros((E, H), jnp.float32), 'v1': jnp.ones((E, H), jnp.float32), 'W2': jax.random.normal(ks[3], (E, H, H), jnp.float32) * s2, 'b2': jnp.zeros((E, H), jnp.float32), 'g2': jnp.ones((E, H), jnp.float32), 'be2': jnp.zeros((E, H), jnp.float32), 'm2': jnp.zeros((E, H), jnp.float32), 'v2': jnp.ones((E, H), jnp.float32), 'Wo': jax.random.normal(ks[4], (E, H, D), jnp.float32) * s2, 'bo': jnp.zeros((E, D), jnp.float32)}
    _L0_ffn_all = _L0_ffn_setup()
    _L0_ffn_in = {k: v for k, v in _L0_ffn_all.items() if k in ('Wr', 'br', 'W1', 'b1', 'g1', 'be1', 'm1', 'v1', 'W2', 'b2', 'g2', 'be2', 'm2', 'v2', 'Wo', 'bo')}
    del _L0_ffn_all
    return {'x': x, 'src': src, 'dst': dst, 'L0_gnn_W': _L0_gnn_in['W'], 'L0_gnn_att_src': _L0_gnn_in['att_src'], 'L0_gnn_att_dst': _L0_gnn_in['att_dst'], 'L0_gnn_bias': _L0_gnn_in['bias'], 'L0_mix_W_qkv': _L0_mix_in['W_qkv'], 'L0_mix_W_out': _L0_mix_in['W_out'], 'L0_mix_b_out': _L0_mix_in['b_out'], 'L0_ffn_Wr': _L0_ffn_in['Wr'], 'L0_ffn_br': _L0_ffn_in['br'], 'L0_ffn_W1': _L0_ffn_in['W1'], 'L0_ffn_b1': _L0_ffn_in['b1'], 'L0_ffn_g1': _L0_ffn_in['g1'], 'L0_ffn_be1': _L0_ffn_in['be1'], 'L0_ffn_m1': _L0_ffn_in['m1'], 'L0_ffn_v1': _L0_ffn_in['v1'], 'L0_ffn_W2': _L0_ffn_in['W2'], 'L0_ffn_b2': _L0_ffn_in['b2'], 'L0_ffn_g2': _L0_ffn_in['g2'], 'L0_ffn_be2': _L0_ffn_in['be2'], 'L0_ffn_m2': _L0_ffn_in['m2'], 'L0_ffn_v2': _L0_ffn_in['v2'], 'L0_ffn_Wo': _L0_ffn_in['Wo'], 'L0_ffn_bo': _L0_ffn_in['bo']}

def reference(x, src, dst, L0_gnn_W, L0_gnn_att_src, L0_gnn_att_dst, L0_gnn_bias, L0_mix_W_qkv, L0_mix_W_out, L0_mix_b_out, L0_ffn_Wr, L0_ffn_br, L0_ffn_W1, L0_ffn_b1, L0_ffn_g1, L0_ffn_be1, L0_ffn_m1, L0_ffn_v1, L0_ffn_W2, L0_ffn_b2, L0_ffn_g2, L0_ffn_be2, L0_ffn_m2, L0_ffn_v2, L0_ffn_Wo, L0_ffn_bo):
    import jax
    import jax.numpy as jnp

    def _L0_gnn_ref(x, edge_index, W, att_src, att_dst, bias):
        import jax, jax.numpy as jnp
        import numpy as np
        N_NODES = 6250
        N_EDGES = 200000
        H_SIZE = 256
        HEADS = 8
        HEAD_DIM = H_SIZE // HEADS
        NEG_SLOPE = 0.2
        'GATConv (concat heads) -> relu -> dropout(eval=identity).\n\n            x: [N, F]; edge_index: [2, E] with (src=row0, dst=row1) meaning message j->i.\n            '
        N = x.shape[0]
        h = jnp.einsum('nf,fhd->nhd', x, W)
        a_src = jnp.sum(h * att_src, axis=-1)
        a_dst = jnp.sum(h * att_dst, axis=-1)
        src = edge_index[0]
        dst = edge_index[1]
        e = jax.nn.leaky_relu(a_src[src] + a_dst[dst], NEG_SLOPE)
        e_max = jax.ops.segment_max(e, dst, num_segments=N)
        e_exp = jnp.exp(e - e_max[dst])
        denom = jax.ops.segment_sum(e_exp, dst, num_segments=N)
        alpha = e_exp / (denom[dst] + 1e-16)
        msg = h[src] * alpha[:, :, None]
        out = jax.ops.segment_sum(msg, dst, num_segments=N)
        out = out.reshape(N, -1) + bias
        return jax.nn.relu(out)

    def _L0_mix_ref(x, W_qkv, W_out, b_out):
        import jax, jax.numpy as jnp
        import numpy as np
        HEADS = 4
        DIM_HEAD = 32
        B, L, D = x.shape
        scale = DIM_HEAD ** (-0.5)
        qkv = jnp.einsum('bld,df->blf', x, W_qkv)
        qkv = qkv.reshape(B, L, 3, HEADS, DIM_HEAD)
        q = jnp.transpose(qkv[:, :, 0], (0, 2, 1, 3)) * scale
        k = jax.nn.softmax(jnp.transpose(qkv[:, :, 1], (0, 2, 1, 3)), axis=2)
        v = jnp.transpose(qkv[:, :, 2], (0, 2, 1, 3))
        context = jnp.einsum('bhld,bhle->bhde', k, v)
        out = jnp.einsum('bhde,bhld->bhle', context, q)
        out = jnp.transpose(out, (0, 2, 1, 3)).reshape(B, L, HEADS * DIM_HEAD)
        return jnp.einsum('blf,fd->bld', out, W_out) + b_out

    def _L0_ffn_ref(x, Wr, br, W1, b1, g1, be1, m1, v1, W2, b2, g2, be2, m2, v2, Wo, bo):
        import jax, jax.numpy as jnp
        import numpy as np
        BN_EPS = 0.001

        def _bn(h, g, b, m, v):
            return g * (h - m) * jax.lax.rsqrt(v + BN_EPS) + b
        feat = jnp.mean(x, axis=0)
        w = jax.nn.softmax(feat @ Wr + br, axis=-1)
        h = jnp.einsum('bfd,edh->bfeh', x, W1) + b1
        h = jax.nn.relu(_bn(h, g1, be1, m1, v1))
        h = jnp.einsum('bfeh,ehk->bfek', h, W2) + b2
        h = jax.nn.relu(_bn(h, g2, be2, m2, v2))
        y = jnp.einsum('bfeh,ehd->bfed', h, Wo) + bo
        return jnp.einsum('bfed,fe->bfd', y, w)
    edge_index = jnp.stack([src, dst])
    xn = _layernorm(x, axis=-1)
    x = x + _L0_gnn_ref(xn, edge_index, L0_gnn_W, L0_gnn_att_src, L0_gnn_att_dst, L0_gnn_bias) + _L0_mix_ref(xn[None], L0_mix_W_qkv, L0_mix_W_out, L0_mix_b_out)[0]
    x = x + _L0_ffn_ref(_layernorm(x, axis=-1)[None], L0_ffn_Wr, L0_ffn_br, L0_ffn_W1, L0_ffn_b1, L0_ffn_g1, L0_ffn_be1, L0_ffn_m1, L0_ffn_v1, L0_ffn_W2, L0_ffn_b2, L0_ffn_g2, L0_ffn_be2, L0_ffn_m2, L0_ffn_v2, L0_ffn_Wo, L0_ffn_bo)[0]
    return x

_drawn_inputs = setup_inputs


def setup_inputs(seed=0):
    import zlib

    import numpy as np

    out = dict(_drawn_inputs(seed))
    spreads = {'L0_gnn_bias': (0.0, 0.1),
     'L0_mix_b_out': (0.0, 0.1),
     'L0_ffn_br': (0.0, 0.1),
     'L0_ffn_b1': (0.0, 0.326),
     'L0_ffn_g1': (1.0, 0.2),
     'L0_ffn_be1': (0.0, 0.328),
     'L0_ffn_m1': (0.0, 0.319),
     'L0_ffn_v1': (1.0, 0.6),
     'L0_ffn_b2': (0.0, 0.1),
     'L0_ffn_g2': (1.0, 0.2),
     'L0_ffn_be2': (0.0, 0.1),
     'L0_ffn_m2': (0.0, 0.1),
     'L0_ffn_v2': (1.0, 0.574),
     'L0_ffn_bo': (0.0, 0.1)}
    factors = {'L0_gnn_att_dst': 11.308}
    for name, (base, spread) in spreads.items():
        noise = np.random.default_rng([zlib.crc32(name.encode()), seed]).standard_normal(out[name].shape)
        drawn = base * np.exp(spread * noise) if base else spread * noise
        out[name] = jnp.asarray(drawn.astype(out[name].dtype))
    for name, factor in factors.items():
        out[name] = (out[name] * factor).astype(out[name].dtype)
    return out
```

```python
from contextlib import ExitStack

import concourse.bass as bass
from concourse import mybir

ALU = mybir.AluOpType
ACT = mybir.ActivationFunctionType
AX = mybir.AxisListType
F32 = mybir.dt.float32
BF16 = mybir.dt.bfloat16
I32 = mybir.dt.int32

P = 128
NODES, EDGES, D = 6250, 200000, 256
HEADS, HD = 8, 32
EXPERTS = 8
W = -(-NODES // P)
CW = 7
CHUNKS = W // CW
TAIL = NODES - (W - 1) * P
J = 8
GROUP = J * P
GROUPS = -(-EDGES // GROUP)
RING = 4
STEPS = GROUPS + W - 1
HC = HD + 1
ROW = HEADS * HC
TROW = ROW + HEADS
PROJ = TROW + HEADS
MD = 128
KVC = 2 * MD + 1
HALF = CW * P // 2
BIG = 1e30
SLOPE = 0.2
LN_EPS, BN_EPS, DEN_EPS = 1e-5, 1e-3, 1e-16
assert W % CW == 0 and GROUPS % RING == 0 and STEPS % 2 == 0


def gps_layer(nc, x, src, dst, dst_last, rows, wproj, wout, wffn, bn, wr, br, bo, table, out):
    ctx = ExitStack()
    with ctx:
        def sb(name, shape, dt=F32):
            return ctx.enter_context(nc.sbuf_tensor(name, shape, dt))

        def sem(name):
            return ctx.enter_context(nc.semaphore(name))

        nodes = sb("nodes", [P, W, ROW])
        arena2 = sb("arena2", [P, 3 * EXPERTS * 2 * D])
        arena3 = sb("arena3", [P, W * KVC])
        qT = sb("qT", [P, W * P])
        o = 0

        def cut(arena, n):
            nonlocal o
            o += n
            return arena[:, o - n:o]
        dst_int = cut(arena2, 3 * GROUPS * J).bitcast(I32).rearrange("p (k t) -> p k t", k=3)
        hrow = cut(arena2, CW * TROW).rearrange("p (k c) -> p k c", k=CW)
        xn = cut(arena2, CW * D).rearrange("p (k c) -> p k c", k=CW)
        xnT = cut(arena2, CW * D).rearrange("p (k a n) -> p k a n", k=CW, a=2)
        wp = cut(arena2, 2 * (PROJ + 3 * MD)).rearrange("p (a c) -> p a c", a=2)
        ring = arena2[:, 0:RING * J * TROW].rearrange("p (s j c) -> p s j c", s=RING, j=J)
        wf = arena2[:, :].rearrange("p (l e a c) -> p l e a c", l=3, e=EXPERTS, a=2)
        kv = arena3[:, :].rearrange("p (w c) -> p w c", c=KVC)
        o = 0
        onehot = cut(arena3, 2 * J * P).rearrange("p (b j d) -> p b j d", b=2, j=J)
        onehotT = cut(arena3, 2 * J * P).rearrange("p (b j e) -> p b j e", b=2, j=J)
        msg = cut(arena3, 2 * J * ROW).rearrange("p (b j c) -> p b j c", b=2, j=J)
        rescaled = cut(arena3, ROW)
        rel = cut(arena3, 2 * J).rearrange("p (b j) -> p b j", b=2)
        as_s = cut(arena3, 2 * J * HEADS).rearrange("p (b n) -> p b n", b=2)
        pen_s = cut(arena3, 2 * J * HEADS).rearrange("p (b n) -> p b n", b=2)
        pen_t = cut(arena3, 2 * P)[0:J * HEADS, :].rearrange("p (b n) -> p b n", b=2)
        scan_s = cut(arena3, 2 * P)[0:J * HEADS, :].rearrange("p (b n) -> p b n", b=2)
        mt = cut(arena3, 2 * J * (HEADS + 1)).rearrange("p (b j c) -> p b j c", b=2, j=J)
        cand = cut(arena3, J * HEADS).rearrange("p (j h) -> p j h", j=J)
        score = cut(arena3, 2 * J * HEADS).rearrange("p (b n) -> p b n", b=2)
        weights = cut(arena3, 2 * J * HEADS).rearrange("p (b n) -> p b n", b=2)
        o = 0
        xn2 = cut(arena3, CW * D).rearrange("p (k c) -> p k c", k=CW)
        xn2T = cut(arena3, CW * D).rearrange("p (a n) -> p a n", a=2)
        h1 = cut(arena3, CW * D).rearrange("p (a n) -> p a n", a=2)
        h2 = cut(arena3, CW * D).rearrange("p (a n) -> p a n", a=2)
        y = cut(arena3, CW * D).rearrange("p (k c) -> p k c", k=CW)
        x_again = cut(arena3, CW * D).rearrange("p (k c) -> p k c", k=CW)
        q_stage = cut(arena3, CW * P).rearrange("p (k c) -> p k c", k=CW)
        gateT = cut(arena3, CW * P)[0:EXPERTS, :]
        gat = h1.rearrange("p a n -> p (a n)").rearrange("p (k c) -> p k c", k=CW)

        dst_f = sb("dst_f", [P, GROUPS * J])
        starts = sb("starts", [P, GROUPS * J], BF16)
        lasts = sb("lasts", [P, GROUPS * J], BF16)
        a_dst = sb("a_dst", [P, W, HEADS])
        run_max = sb("run_max", [P, W, HEADS])
        shift = sb("shift", [P, W, HEADS])
        ident = sb("ident", [P, P])
        ones = sb("ones", [P, P])
        iota = sb("iota", [P, STEPS])
        thr = sb("thr", [P, 2])
        b_out = sb("b_out", [1, D])
        bias = sb("bias", [P, D])
        one_cols = sb("one_cols", [P, TROW])
        eps = sb("eps", [P, 2])
        o = 0
        row_in = cut(qT, 3 * D)[0:1, :]
        dl_int = cut(qT, GROUPS).bitcast(I32)[0:1, :]
        dl_f = cut(qT, GROUPS)[0:1, :]
        cmp = cut(qT, STEPS + GROUPS)
        use_t = cut(qT, GROUPS)[0:1, :]
        att_tmp = cut(qT, D)
        first = sb("first", [P, 2])
        base = sb("base", [P, STEPS])
        win_i = sb("win_i", [1, STEPS], I32)
        grp_i = sb("grp_i", [1, STEPS], I32)
        use_i = sb("use_i", [1, GROUPS], I32)
        stats = sb("stats", [P, CW, 6])
        mv = sb("mv", [P, CW, 2])
        sd = sb("sd", [P, CW])
        rstd = sb("rstd", [P, CW])
        k_max = sb("k_max", [P, MD])
        k_col = sb("k_col", [P, 1])
        k_diag = sb("k_diag", [P, MD])
        k_exp = sb("k_exp", [P, 2, MD])
        z_inv = sb("z_inv", [P, 1])
        ctx_n = sb("ctx_n", [P, MD])
        ctx_t = sb("ctx_t", [P, MD])
        w_o = sb("w_o", [P, D])
        mixer = sb("mixer", [P, D])
        idx = sb("idx", [P, RING, J], I32)
        absent = sb("absent", [P, J])
        gmax = sb("gmax", [P, HEADS])
        zc = sb("zc", [P, HEADS])
        adc = sb("adc", [P, 2, 2 * HEADS])
        grew = sb("grew", [P, 2, HEADS])
        factor = sb("factor", [P, 2, HEADS])
        bnp = sb("bnp", [P, 5, 2, 2 * EXPERTS])
        bns = sb("bns", [P, 3, 2, 2 * EXPERTS])
        w_r = sb("w_r", [P, 2, EXPERTS])
        b_r = sb("b_r", [1, EXPERTS])
        b_o = sb("b_o", [EXPERTS, D])
        inv = sb("inv", [P, CW, HEADS])
        mv2 = sb("mv2", [P, W, 2])
        rstd2 = sb("rstd2", [P, W])
        lg = sb("lg", [P, CW, EXPERTS])
        lmax = sb("lmax", [P, CW])
        lsum = sb("lsum", [P, CW])
        gate = sb("gate", [P, CW, EXPERTS])

        ps = ctx.enter_context(nc.psum_tensor("ps", [P, 8, 512], F32))

        s_x = [sem(f"s_x{i}") for i in range(CHUNKS)]
        s_in = sem("s_in")
        s_dst = sem("s_dst")
        s_xready = sem("s_xready")
        s_const = sem("s_const")
        s_dc = sem("s_dc")
        s_pc = sem("s_pc")
        s_stat = sem("s_stat")
        s_mv = sem("s_mv")
        s_sd = sem("s_sd")
        s_rs = sem("s_rs")
        s_xn = sem("s_xn")
        s_xt = sem("s_xt")
        s_xte = sem("s_xte")
        s_h = sem("s_h")
        s_kv = sem("s_kv")
        s_q = sem("s_q")
        s_hrow = sem("s_hrow")
        s_ad = sem("s_ad")
        s_kve = sem("s_kve")
        s_qe = sem("s_qe")
        s_hst = [sem(f"s_hst{k}") for k in range(CW)]
        s_hfree = sem("s_hfree")
        s_kd = sem("s_kd")
        s_kp = sem("s_kp")
        s_ke = sem("s_ke")
        s_ks = sem("s_ks")
        s_kc = sem("s_kc")
        s_bnr = sem("s_bnr")
        s_idx = [sem(f"s_idx{k}") for k in range(RING)]
        s_gat = [sem(f"s_gat{k}") for k in range(RING)]
        s_seen = sem("s_seen")
        s_gathered = sem("s_gathered")
        s_as = sem("s_as")
        s_rel = sem("s_rel")
        s_oh = sem("s_oh")
        s_pen = sem("s_pen")
        s_ast = sem("s_ast")
        s_ohp = sem("s_ohp")
        s_pent = sem("s_pent")
        s_oht = sem("s_oht")
        s_scan = sem("s_scan")
        s_back = sem("s_back")
        s_mt = sem("s_mt")
        s_pm = sem("s_pm")
        s_ch = sem("s_ch")
        s_ade = sem("s_ade")
        s_sc = sem("s_sc")
        s_fac = sem("s_fac")
        s_w = sem("s_w")
        s_msg = sem("s_msg")
        s_seg = sem("s_seg")
        s_acc = sem("s_acc")
        s_wf = sem("s_wf")
        s_xa = sem("s_xa")
        s_qs = sem("s_qs")
        s_mix = sem("s_mix")
        s_r = sem("s_r")
        s_sd2 = sem("s_sd2")
        s_rs2 = sem("s_rs2")
        s_n2 = sem("s_n2")
        s_t2 = sem("s_t2")
        s_t2e = sem("s_t2e")
        s_lg = sem("s_lg")
        s_g = sem("s_g")
        s_ge = sem("s_ge")
        s_gt = sem("s_gt")
        s_gte = sem("s_gte")
        s_l = sem("s_l")
        s_le = sem("s_le")
        s_l3 = sem("s_l3")
        s_y = sem("s_y")
        s_out = sem("s_out")
        s_yfree = sem("s_yfree")

        CH = 9
        RS = 6 + 2 * CW + 1
        LT = 8 * EXPERTS
        YT = (EXPERTS + 1) * CW

        def settle(engine):
            engine.sem_inc(s_seen, 1)
        block = ctx.enter_context(nc.Block())

        x_t = x.rearrange("(w p) c -> p w c", p=P)
        out_t = out.rearrange("(w p) c -> p w c", p=P)

        @block.sync
        def _(sp):
            for i in range(CHUNKS):
                sp.dma_start(nodes[:, i * CW:(i + 1) * CW, 0:D], x_t[:, i * CW:(i + 1) * CW, :]).then_inc(s_x[i], 16)
                if i == 0:
                    sp.dma_start(dst_int, dst).then_inc(s_dst, 16)
            for i in range(CHUNKS):
                sp.wait_ge(s_x[i], 16)
                sp.sem_inc(s_xready, 1)
            sp.sem_inc(s_hfree, 1)
            with sp.Fori(0, CHUNKS) as i:
                for k in range(CW):
                    sp.wait_ge(s_hrow, i * CW + k + 1)
                    sp.dma_start(table[bass.ds(i * (CW * P) + k * P, P), :], hrow[:, k, :]).then_inc(s_hst[k], 16)
                for k in range(CW):
                    sp.wait_ge(s_hst[k], i * 16 + 16)
                sp.sem_inc(s_hfree, 1)
            for k in range(RING):
                sp.dma_start(idx[:, k, :], src[k, :, :]).then_inc(s_idx[k], 16)
            for k in range(2):
                sp.wait_ge(s_gat[k], 16 * J)
                sp.sem_inc(s_gathered, 1)
            sp.wait_ge(s_dc, SETUP_DONE)
            with sp.Fori(RING, GROUPS - RING + 1, RING) as g:
                for k in range(RING):
                    sp.wait_ge(s_gat[(k + 2) % RING], g * (16 * J // RING) + (16 * J if k >= 2 else 0))
                    sp.sem_inc(s_gathered, 1)
                    used = sp.value_load(use_i[0:1, bass.ds(g + (k - RING), 1)], min_val=1, max_val=4 * STEPS)
                    sp.wait_ge(s_msg, used)
                    sp.dma_start(idx[:, k, :].unsqueeze(1), src[bass.ds(g + k, 1), :, :].rearrange("g p j -> p g j")).then_inc(s_idx[k], 16)
            for k in range(2):
                sp.wait_ge(s_gat[2 + k], 16 * J * GROUPS // RING)
                sp.sem_inc(s_gathered, 1)
            sp.wait_ge(s_msg, 4 * STEPS)
            sp.dma_start(arena2[:, :], wffn).then_inc(s_wf, 16)
            sp.wait_ge(s_acc, 4 + 2 * STEPS)
            sp.wait_ge(s_seg, STEPS)
            with sp.Fori(0, CHUNKS) as i:
                sp.dma_start(x_again, x_t[:, bass.ds(i * CW, CW), :]).then_inc(s_xa, 16)
                sp.wait_ge(s_r, i * RS + 6)
                settle(sp)
            sp.sem_inc(s_yfree, 1)
            with sp.Fori(0, CHUNKS) as c:
                sp.wait_ge(s_y, 3 + c * YT + YT)
                sp.dma_start(out_t[:, bass.ds(c * CW, CW), :], y).then_inc(s_out, 16)
                sp.wait_ge(s_out, c * 16 + 16)
                sp.sem_inc(s_yfree, 1)

        @block.gpsimd
        def _(pool):
            pool.memset(ident[:], 0.0).then_inc(s_const, 1)
            pool.memset(ones[:], 1.0).then_inc(s_const, 1)
            pool.memset(kv[:, :, 2 * MD:KVC], 1.0).then_inc(s_const, 1)
            pool.memset(eps[:, 0:1], LN_EPS).then_inc(s_const, 1)
            pool.memset(eps[:, 1:2], BN_EPS).then_inc(s_const, 1)
            pool.iota(iota[:], pattern=[[1, STEPS]], base=0, channel_multiplier=0,
                      allow_small_or_imprecise_dtypes=True).then_inc(s_const, 1)
            pool.iota(thr[:, 0:1], pattern=[[0, 1]], base=1, channel_multiplier=1,
                      allow_small_or_imprecise_dtypes=True).then_inc(s_const, 1)
            pool.iota(thr[:, 1:2], pattern=[[0, 1]], base=P, channel_multiplier=P,
                      allow_small_or_imprecise_dtypes=True).then_inc(s_const, 1)
            pool.wait_ge(s_const, 8)
            pool.affine_select(out=ident[:], in_=ident[:], compare_op=ALU.not_equal, fill=1.0, base=0,
                               pattern=[[-1, P]], channel_multiplier=1).then_inc(s_const, 1)
            pool.affine_select(out=kv[:, W - 1, 2 * MD:KVC], in_=kv[:, W - 1, 2 * MD:KVC], compare_op=ALU.is_ge,
                               fill=0.0, base=TAIL - 1, pattern=[[0, 1]], channel_multiplier=-1).then_inc(s_const, 1)
            for k in range(CW):
                pool.wait_ge(s_hst[k], 16 * CHUNKS)
            pool.wait_ge(s_kv, W)
            pool.wait_ge(s_q, W)
            with pool.Fori(0, GROUPS - RING + 1, RING) as g:
                for k in range(RING):
                    pool.wait_ge(s_idx[k], g * (16 // RING) + 16)
                    settle(pool)
                    for j in range(J):
                        pool.indirect_dma_start(
                            out=ring[:, k, j, :], out_offset=None, in_=table,
                            in_offset=bass.IndirectOffsetOnAxis(ap=idx[:, k, j:j + 1], axis=0)).then_inc(s_gat[k], 16)

        @block.scalar
        def _(act):
            for dest, source in ((row_in, rows[:, 0:3 * D]), (b_out[:], rows[:, 3 * D:]), (wp, wproj), (dl_int, dst_last), (w_o[:], wout),
                                 (bnp[:], bn), (w_r[:], wr), (b_r[:], br), (b_o[:], bo)):
                act.dma_start(dest, source).then_inc(s_in, 16)
            act.wait_ge(s_in, 16 * 9)
            act.wait_ge(s_const, 10)
            act.activation(bns[:, 2, :, :], bnp[:, 4, :, :], ACT.Sqrt, bias=eps[:, 1:2]).then_inc(s_bnr, 1)
            act.sem_inc(s_xte, 2)
            act.sem_inc(s_kve, 2)
            act.sem_inc(s_ad, 2)
            with act.Fori(0, CHUNKS) as i:
                act.wait_ge(s_mv, i * CW + CW)
                act.activation(sd[:].unsqueeze(2), mv[:, :, 1:2], ACT.Sqrt, bias=eps[:, 0:1]).then_inc(s_sd, 1)
                for k in range(CW):
                    w = i * CW + k
                    act.wait_ge(s_xt, w + 1)
                    act.activation(xnT[:, k, :, :], ps[:, k % 2, 0:D].rearrange("p (a n) -> p a n", a=2),
                                   ACT.Copy).then_inc(s_xte, 1)
                    act.wait_ge(s_hrow, w + 1)
                    act.activation(a_dst[:, bass.ds(w, 1), :], ps[:, 2 + k % 2, TROW:PROJ].unsqueeze(1),
                                   ACT.Copy).then_inc(s_ad, 1)
                    act.wait_ge(s_kv, w + 1)
                    act.activation(kv[:, bass.ds(w, 1), 0:2 * MD], ps[:, 4 + k % 2, 0:2 * MD].unsqueeze(1),
                                   ACT.Copy).then_inc(s_kve, 1)
            act.sem_inc(s_ke, 2)
            with act.Fori(0, CHUNKS) as i:
                act.wait_ge(s_ks, i + 1)
                for k in range(CW):
                    w = i * CW + k
                    back = {0: 1, 1: 3}.get(k, 2)
                    act.wait_ge(s_kc, w + 3 - back)
                    act.activation(k_exp[:, k % 2, :].unsqueeze(1), kv[:, bass.ds(w, 1), 0:MD], ACT.Exp).then_inc(s_ke, 1)
            act.wait_ge(s_kd, CTX_DONE)
            act.sem_inc(s_oht, 1)

            def shift_rows(s, b):
                g = act.value_load(grp_i[0:1, bass.ds(s, 1)], min_val=0, max_val=GROUPS - 1)
                act.wait_ge(s_gathered, g + 1)
                act.wait_ge(s_sc, 4 * s + 4)
                act.activation(as_s[:, b, :].rearrange("p (o j h) -> p o j h", o=1, j=J),
                               ring[:, bass.ds(g % RING, 1), :, ROW:TROW], ACT.Copy).then_inc(s_as, 1)

            def exps(s, b):
                act.wait_ge(s_ch, CH * s + 8)
                act.activation(factor[:, b, :], grew[:, b, :], ACT.Exp).then_inc(s_fac, 1)
                act.wait_ge(s_sc, 8 + 4 * s + 4)
                act.activation(weights[:, b, :], score[:, b, :], ACT.Exp).then_inc(s_w, 1)

            def evacuate(s, b):
                act.wait_ge(s_ast, s + 1)
                act.activation(pen_t[:, b, :], ps[0:J * HEADS, 4 + b, P:2 * P], ACT.Copy).then_inc(s_pent, 1)
                act.wait_ge(s_ohp, s + 1)
                act.activation(onehotT[:, b, :, :].rearrange("p j e -> p (j e)"),
                               ps[:, 0:2, :].rearrange("p b n -> p (b n)"), ACT.Copy).then_inc(s_oht, 1)
            for s in range(2):
                shift_rows(s, s)
                evacuate(s, s)
            exps(0, 0)
            with act.Fori(0, STEPS - 3, 2) as t:
                for b in range(2):
                    s = t + b
                    shift_rows(s + 2, b)
                    exps(s + 1, 1 - b)
                    evacuate(s + 2, b)
            exps(STEPS - 1, 1)
            act.wait_ge(s_acc, 4 + 2 * STEPS)
            with act.Fori(0, CHUNKS) as i:
                for k in range(CW):
                    act.wait_ge(s_mix, i * CW + k + 1)
                    act.activation(q_stage[:, k, :], qT[:, bass.ds((i * CW + k) * P, P)], ACT.Copy).then_inc(s_qs, 1)
            act.wait_ge(s_r, 1 + CHUNKS * RS)
            act.activation(rstd2[:].unsqueeze(2), mv2[:, :, 1:2], ACT.Sqrt, bias=eps[:, 0:1]).then_inc(s_sd2, 1)
            act.sem_inc(s_le, 4)
            with act.Fori(0, CHUNKS) as c:
                for k in range(CW):
                    act.wait_ge(s_t2, c * CW + k + 1)
                    act.activation(xn2T[:, :, k * P:(k + 1) * P],
                                   ps[:, k % 4, 0:D].rearrange("p (a n) -> p a n", a=2),
                                   ACT.Copy).then_inc(s_t2e, 1)
                act.wait_ge(s_g, c * 5 + 2)
                act.activation(lg[:], lg[:], ACT.Exp).then_inc(s_ge, 1)
                act.wait_ge(s_gt, c + 1)
                act.activation(gateT, ps[0:EXPERTS, 2:4, :].rearrange("p b n -> p (b n)")[:, 0:CW * P],
                               ACT.Copy).then_inc(s_gte, 1)
                for e in range(EXPERTS):
                    for n, (layer, half, m) in enumerate((l, a, m) for l in range(2) for a in range(2) for m in range(2)):
                        act.wait_ge(s_l, c * LT + (8 * e + n + 1))
                        dest = (h1, h2)[layer][:, m, half * HALF:(half + 1) * HALF]
                        col = 2 * e + m
                        act.activation(dest, ps[:, n % 4, 0:HALF], ACT.Relu, bias=bns[:, 1, layer, col:col + 1],
                                       scale=bns[:, 0, layer, col:col + 1]).then_inc(s_le, 1)

        @block.tensor
        def _(pe):
            pe.wait_ge(s_in, 16 * 9)
            pe.wait_ge(s_const, 10)
            pe.matmul(ps[:, 0, :], ones[0:1, :], row_in[:, 0:2 * D], start=True, stop=True)
            pe.matmul(ps[:, 1, 0:D], ones[0:1, :], row_in[:, 2 * D:3 * D], start=True, stop=True).then_inc(s_pc, 1)
            pe.wait_ge(s_dc, 1)
            pe.matmul(ps[0:W - 1, 2, 0:GROUPS], ones[0:1, 0:W - 1], dl_f, start=True, stop=True).then_inc(s_pc, 1)
            pe.wait_ge(s_dc, STEP_TABLES)
            pe.matmul(ps[:, 3, 0:STEPS + GROUPS], ones[0:W - 1, :], cmp[0:W - 1, :], start=True, stop=True).then_inc(s_pc, 1)
            pe.wait_ge(s_dc, SETUP_DONE)
            with pe.Fori(0, CHUNKS) as i:
                for k in range(CW):
                    w = i * CW + k
                    back = {0: 1, 1: 3}.get(k, 2)
                    pe.wait_ge(s_xn, w + 1)
                    pe.wait_ge(s_xte, w + 3 - back)
                    for a in range(2):
                        mm = pe.transpose(ps[:, k % 2, a * P:(a + 1) * P], xn[:, k, a * P:(a + 1) * P], ident[:])
                    mm.then_inc(s_xt, 1)
                    pe.wait_ge(s_xte, 2 + w + 1)
                    pe.wait_ge(s_ad, w + 3 - back)
                    for a in range(2):
                        mm = pe.matmul(ps[:, 2 + k % 2, 0:PROJ], xnT[:, k, a, :], wp[:, a, 0:PROJ], start=(a == 0), stop=(a == 1))
                    mm.then_inc(s_h, 1)
                    pe.wait_ge(s_kve, w + 3 - back)
                    for a in range(2):
                        mm = pe.matmul(ps[:, 4 + k % 2, 0:2 * MD], xnT[:, k, a, :], wp[:, a, PROJ:PROJ + 2 * MD], start=(a == 0), stop=(a == 1))
                    mm.then_inc(s_kv, 1)
                    pe.wait_ge(s_qe, w + 3 - back)
                    for a in range(2):
                        mm = pe.matmul(ps[:, 6 + k % 2, 0:P], wp[:, a, PROJ + 2 * MD:], xnT[:, k, a, :], start=(a == 0), stop=(a == 1))
                    mm.then_inc(s_q, 1)
            pe.wait_ge(s_kd, 2)
            pe.transpose(ps[:, 0, 0:MD], k_max[:], ident[:]).then_inc(s_kp, 1)
            pe.wait_ge(s_kd, 4)
            pe.matmul(ps[:, 1, 0:MD], ones[:], k_diag[:], start=True, stop=True).then_inc(s_kp, 1)
            pe.wait_ge(s_kd, 5)
            pe.matmul(ps[:, 2, 0:MD + 1], ident[:], one_cols[:, 0:MD + 1], start=True, stop=False)
            pe.sem_inc(s_kc, 2)
            with pe.Fori(0, CHUNKS) as i:
                for k in range(CW):
                    w = i * CW + k
                    pe.wait_ge(s_ke, 2 + w + 1)
                    pe.matmul(ps[:, 2, 0:MD + 1], k_exp[:, k % 2, :],
                              kv[:, bass.ds(w, 1), MD:KVC].rearrange("p w c -> p (w c)"),
                              start=False, stop=False).then_inc(s_kc, 1)
            pe.matmul(ps[:, 2, 0:MD + 1], ident[:], one_cols[:, 0:MD + 1], start=False, stop=True).then_inc(s_kp, 1)
            pe.wait_ge(s_kd, CTX_DONE - 2)
            pe.transpose(ps[:, 3, 0:MD], ctx_n[:], ident[:]).then_inc(s_kp, 1)
            pe.wait_ge(s_kd, CTX_DONE - 1)
            pe.matmul(ps[:, 4, 0:D], ctx_t[:], w_o[:], start=True, stop=True).then_inc(s_kp, 1)
            pe.wait_ge(s_kd, CTX_DONE)

            def turn(s, b):
                pe.wait_ge(s_as, s + 1)
                pe.wait_ge(s_pen, s + 1)
                pe.wait_ge(s_scan, s + 1)
                settle(pe)
                pe.transpose(ps[0:J * HEADS, 4 + b, 0:P], as_s[:, b, :], ident[:])
                pe.transpose(ps[0:J * HEADS, 4 + b, P:2 * P], pen_s[:, b, :], ident[:]).then_inc(s_ast, 1)
                pe.wait_ge(s_oh, s + 1)
                pe.wait_ge(s_oht, s + 1)
                for j in range(J):
                    mm = pe.transpose(ps[:, j // 4, (j % 4) * P:(j % 4 + 1) * P], onehot[:, b, j, :], ident[:])
                mm.then_inc(s_ohp, 1)

            def maxima_back(s, b):
                pe.wait_ge(s_scan, 2 + s + 1)
                pe.wait_ge(s_mt, 2 * s + 2)
                settle(pe)
                pe.transpose(ps[:, 4 + b, 256:256 + J * HEADS], scan_s[:, b, :], ident[0:J * HEADS, 0:J * HEADS]).then_inc(s_back, 1)

            def maxima_by_node(s, b):
                pe.wait_ge(s_mt, 4 + 2 * s + 2)
                for j in range(J):
                    mm = pe.matmul(ps[:, 4 + b, 384 + 9 * j:384 + 9 * j + 9], onehot[:, b, j, :], mt[:, b, j, :], start=True, stop=True)
                mm.then_inc(s_pm, 1)

            def to_edges(s, b):
                pe.wait_ge(s_ch, CH * s + 7)
                pe.wait_ge(s_oht, 1 + s + 1)
                for j in range(J):
                    mm = pe.matmul(ps[:, 6, 128 * b + 16 * j:128 * b + 16 * j + 16], onehotT[:, b, j, :], adc[:, b, :], start=True, stop=True)
                mm.then_inc(s_ade, 1)

            def sums(s, b, q):
                pe.wait_ge(s_msg, 4 * s + (q + 1))
                if q == 0:
                    pe.wait_ge(s_acc, 2 * s + 2)
                for j in (2 * q, 2 * q + 1):
                    mm = pe.matmul(ps[:, 2 + b, 0:ROW], onehot[:, b, j, :], msg[:, b, j, :], start=(j == 0), stop=(j == J - 1))
                if q == 3:
                    mm.then_inc(s_seg, 1)
            for s in range(2):
                turn(s, s)
            maxima_back(0, 0)
            maxima_by_node(0, 0)
            to_edges(0, 0)

            def step(s, b, nxt=True, after=True):
                if nxt:
                    maxima_back(s + 1, 1 - b)
                sums(s, b, 0)
                if nxt:
                    maxima_by_node(s + 1, 1 - b)
                sums(s, b, 1)
                if nxt:
                    to_edges(s + 1, 1 - b)
                sums(s, b, 2)
                sums(s, b, 3)
                if after:
                    turn(s + 2, b)
            with pe.Fori(0, STEPS - 3, 2) as t:
                for b in range(2):
                    step(t + b, b)
            step(STEPS - 2, 0, True, False)
            step(STEPS - 1, 1, False, False)
            pe.sem_inc(s_mix, CW)
            with pe.Fori(0, CHUNKS) as i:
                for k in range(CW):
                    pe.wait_ge(s_qs, i * CW + k + 1)
                    if k == 0:
                        pe.wait_ge(s_r, 1 + i * RS)
                    dest = ps[:, k // 2, 256 * (k % 2):256 * (k % 2) + 256]
                    pe.matmul(dest, q_stage[:, k, :], mixer[:], start=True, stop=False)
                    pe.matmul(dest, ones[0:1, :], b_out[:], start=False, stop=True).then_inc(s_mix, 1)
            pe.wait_ge(s_wf, 16)
            pe.wait_ge(s_r, 1 + CHUNKS * RS)
            with pe.Fori(0, CHUNKS) as c:
                for k in range(CW):
                    pe.wait_ge(s_n2, c * CW + k + 1)
                    if k >= 4:
                        pe.wait_ge(s_t2e, c * CW + k - 3)
                    for a in range(2):
                        mm = pe.transpose(ps[:, k % 4, a * P:(a + 1) * P], xn2[:, k, a * P:(a + 1) * P], ident[:])
                    mm.then_inc(s_t2, 1)
                pe.wait_ge(s_t2e, c * CW + CW)
                for k in range(CW):
                    dest = ps[:, 7, 8 * k:8 * k + 8]
                    for a in range(2):
                        pe.matmul(dest, xn2T[:, a, k * P:(k + 1) * P], w_r[:, a, :], start=(a == 0), stop=False)
                    mm = pe.matmul(dest, ones[0:1, :], b_r[:], start=False, stop=True)
                mm.then_inc(s_lg, 1)
                pe.wait_ge(s_g, c * 5 + 5)
                for k in range(CW):
                    mm = pe.transpose(ps[0:EXPERTS, 2 + k // 4, (k % 4) * P:(k % 4 + 1) * P], gate[:, k, :], ident[:])
                mm.then_inc(s_gt, 1)
                pe.wait_ge(s_gte, c + 1)

                def y_tile(n, k, terms):
                    pe.wait_ge(s_y, c * YT + (n + 1))
                    for t, (a, b) in enumerate(terms):
                        mm = pe.matmul(ps[:, 4 + n % 3, 0:D], a, b, start=(t == 0), stop=(t == len(terms) - 1))
                    mm.then_inc(s_l3, 1)
                for k in range(CW):
                    y_tile(k, k, [(gateT[:, k * P:(k + 1) * P], b_o[:])])
                for e in range(EXPERTS):
                    for n, (layer, half, m) in enumerate((l, a, m) for l in range(2) for a in range(2) for m in range(2)):
                        i12 = 8 * e + n
                        pe.wait_ge(s_le, c * LT + (i12 + 1))
                        if layer:
                            pe.wait_ge(s_le, c * LT + (8 * e + 2 * half + 2 + 4))
                        rhs = (xn2T, h1)[layer]
                        for a in range(2):
                            mm = pe.matmul(ps[:, n % 4, 0:HALF], wf[:, layer, e, a, m * P:(m + 1) * P],
                                           rhs[:, a, half * HALF:(half + 1) * HALF], start=(a == 0), stop=(a == 1))
                        mm.then_inc(s_l, 1)
                    for k in range(CW):
                        pe.wait_ge(s_le, c * LT + (8 * e + (6 if k < 3 else 8) + 4))
                        y_tile(CW * (e + 1) + k, k, [(h2[:, a, k * P:(k + 1) * P], wf[:, 2, e, a, :]) for a in range(2)])

        @block.vector
        def _(dve):
            n_dc = [0]

            def done(ins):
                n_dc[0] += 1
                ins.then_inc(s_dc, 1)
                dve.wait_ge(s_dc, n_dc[0])
            dve.wait_ge(s_in, 16 * 9)
            dve.wait_ge(s_const, 10)
            done(dve.tensor_copy(dl_f, dl_int))
            dve.wait_ge(s_pc, 2)
            done(dve.tensor_scalar(cmp[0:W - 1, 0:GROUPS], ps[0:W - 1, 2, 0:GROUPS], thr[0:W - 1, 1:2], None, ALU.is_lt))
            done(dve.tensor_reduce(first[0:W - 1, 0:1], cmp[0:W - 1, 0:GROUPS], AX.X, ALU.add))
            done(dve.tensor_tensor(first[0:W - 1, 1:2], first[0:W - 1, 0:1], thr[0:W - 1, 0:1], ALU.add))
            done(dve.tensor_scalar(cmp[0:W - 1, 0:STEPS], iota[0:W - 1, :], first[0:W - 1, 1:2], None, ALU.is_ge))
            done(dve.tensor_scalar(cmp[0:W - 1, STEPS:], iota[0:W - 1, 0:GROUPS], first[0:W - 1, 0:1], None, ALU.is_ge))
            assert n_dc[0] == STEP_TABLES
            dve.wait_ge(s_dst, 16)
            done(dve.tensor_copy(dst_f[:], dst_int[:, 0, :]))
            done(dve.tensor_tensor(starts[:], dst_int[:, 0, :], dst_int[:, 1, :], ALU.not_equal))
            done(dve.tensor_tensor(lasts[:], dst_int[:, 0, :], dst_int[:, 2, :], ALU.not_equal))
            dve.wait_ge(s_pc, 3)
            done(dve.tensor_scalar(base[:], ps[:, 3, 0:STEPS], float(P), None, ALU.mult))
            done(dve.tensor_copy(win_i[:], ps[0:1, 3, 0:STEPS]))
            done(dve.tensor_tensor(grp_i[:], iota[0:1, :], ps[0:1, 3, 0:STEPS], ALU.subtract))
            done(dve.tensor_tensor(use_t, iota[0:1, 0:GROUPS], ps[0:1, 3, STEPS:STEPS + GROUPS], ALU.add))
            done(dve.tensor_scalar(use_i[:], use_t, 1.0, 4.0, ALU.add, ALU.mult))
            done(dve.tensor_copy(bias[:], ps[:, 1, 0:D]))
            for a in range(2):
                w_h = wp[:, a, 0:ROW].rearrange("p (h c) -> p h c", c=HC)[:, :, 0:HD]
                for t in range(2):
                    done(dve.tensor_tensor(att_tmp.rearrange("p (h c) -> p h c", c=HD), w_h,
                                           ps[:, 0, t * D:(t + 1) * D].rearrange("p (h c) -> p h c", c=HD), ALU.mult))
                    done(dve.tensor_reduce(wp[:, a, ROW + t * HEADS:ROW + (t + 1) * HEADS],
                                           att_tmp.rearrange("p (h c) -> p h c", c=HD), AX.X, ALU.add))
            done(dve.memset(one_cols[:], 0.0))
            done(dve.memset(one_cols[:, 0:ROW].rearrange("p (h c) -> p h c", c=HC)[:, :, HD:HC], 1.0))
            dve.wait_ge(s_bnr, 1)
            done(dve.reciprocal(bns[:, 2, :, :], bns[:, 2, :, :]))
            done(dve.tensor_tensor(bns[:, 0, :, :], bnp[:, 1, :, :], bns[:, 2, :, :], ALU.mult))
            done(dve.tensor_tensor(bns[:, 1, :, :], bnp[:, 0, :, :], bnp[:, 3, :, :], ALU.subtract))
            done(dve.tensor_tensor(bns[:, 1, :, :], bns[:, 1, :, :], bns[:, 0, :, :], ALU.mult))
            done(dve.tensor_tensor(bns[:, 1, :, :], bns[:, 1, :, :], bnp[:, 2, :, :], ALU.add))
            done(dve.memset(run_max[:], -BIG))
            done(dve.memset(shift[:], -BIG))
            assert n_dc[0] == SETUP_DONE
            dve.sem_inc(s_qe, 2)
            with dve.Fori(0, CHUNKS) as i:
                dve.wait_ge(s_xready, i + 1)
                for k in range(CW):
                    dve.bn_stats(stats[:, k, :], nodes[:, bass.ds(i * CW + k, 1), 0:D].rearrange("p w c -> p (w c)")).then_inc(s_stat, 1)
                dve.wait_ge(s_stat, i * CW + CW)
                settle(dve)
                for k in range(CW):
                    dve.bn_aggr(mv[:, k, :], stats[:, k, :]).then_inc(s_mv, 1)
                dve.wait_ge(s_sd, i + 1)
                dve.reciprocal(rstd[:], sd[:]).then_inc(s_rs, 1)
                dve.wait_ge(s_rs, i + 1)
                dve.wait_ge(s_mv, i * CW + CW)
                for k in range(CW):
                    dve.tensor_scalar(xn[:, k, :].unsqueeze(1), nodes[:, bass.ds(i * CW + k, 1), 0:D], mv[:, k, 0:1], rstd[:, k:k + 1],
                                      ALU.subtract, ALU.mult).then_inc(s_xn, 1)
                dve.wait_ge(s_hfree, i + 1)
                for k in range(CW):
                    w = i * CW + k
                    dve.wait_ge(s_h, w + 1)
                    dve.tensor_tensor(hrow[:, k, :], ps[:, 2 + k % 2, 0:TROW], one_cols[:], ALU.add).then_inc(s_hrow, 1)
                    dve.wait_ge(s_q, w + 1)
                    dve.tensor_scalar(qT[:, bass.ds(w * P, P)], ps[:, 6 + k % 2, 0:P], 1.0, None, ALU.mult).then_inc(s_qe, 1)
            n_kd = [0]

            def kd(ins):
                n_kd[0] += 1
                ins.then_inc(s_kd, 1)
                dve.wait_ge(s_kd, n_kd[0])
            dve.wait_ge(s_kve, 2 + W)
            kd(dve.tensor_reduce(k_max[:], kv[:, 0:W - 1, 0:MD].rearrange("p w c -> p c w"), AX.X, ALU.max))
            kd(dve.tensor_tensor(k_max[0:TAIL, :], k_max[0:TAIL, :], kv[0:TAIL, W - 1, 0:MD], ALU.max))
            dve.wait_ge(s_kp, 1)
            kd(dve.tensor_reduce(k_col[:], ps[:, 0, 0:MD], AX.X, ALU.max))
            kd(dve.tensor_scalar(k_diag[:], ident[:], k_col[:, 0:1], None, ALU.mult))
            kd(dve.memset(one_cols[:], 0.0))
            dve.wait_ge(s_kp, 2)
            with dve.Fori(0, CHUNKS) as i:
                part = kv[:, bass.ds(i * CW, CW), 0:MD]
                dve.tensor_tensor(part, part, ps[:, 1, 0:MD].unsqueeze(1).to_broadcast([P, CW, MD]), ALU.subtract).then_inc(s_ks, 1)
            kd(dve.memset(nodes[:], 0.0))
            kd(dve.memset(ctx_n[:], 0.0))
            dve.wait_ge(s_kp, 3)
            kd(dve.reciprocal(z_inv[:], ps[:, 2, MD:MD + 1]))
            for h in range(4):
                r = slice(32 * h, 32 * h + 32)
                kd(dve.tensor_scalar(ctx_n[r, r], ps[r, 2, r], z_inv[r, 0:1], float(HD) ** -0.5, ALU.mult, ALU.mult))
            assert n_kd[0] == CTX_DONE - 2
            dve.wait_ge(s_kp, 4)
            kd(dve.tensor_copy(ctx_t[:], ps[:, 3, 0:MD]))
            dve.wait_ge(s_kp, 5)
            kd(dve.tensor_copy(mixer[:], ps[:, 4, 0:D]))
            assert n_kd[0] == CTX_DONE
            dve.wait_ge(s_kc, 2 + W)

            dve.sem_inc(s_sc, 8)
            dve.sem_inc(s_scan, 2)
            dve.sem_inc(s_mt, 4)
            dve.sem_inc(s_acc, 4)

            def load(tab, s, high):
                return dve.value_load(tab[0:1, bass.ds(s, 1)], min_val=0, max_val=high)

            def make_onehot(s, b):
                g = load(grp_i, s, GROUPS - 1)
                dve.tensor_scalar(rel[:, b, :], dst_f[:, bass.ds(g * J, J)], base[:, bass.ds(s, 1)], None,
                                  ALU.subtract).then_inc(s_rel, 1)
                if not isinstance(s, int):
                    dve.wait_ge(s_ast, s - 1)
                dve.tensor_scalar(pen_s[:, b, :].rearrange("p (j h) -> p j h", j=J),
                                  starts[:, bass.ds(g * J, J)].unsqueeze(2).to_broadcast([P, J, HEADS]), -BIG, None,
                                  ALU.mult).then_inc(s_pen, 1)
                dve.wait_ge(s_rel, s + 1)
                dve.tensor_tensor(onehot[:, b, :, :], iota[:, 0:P].unsqueeze(1).to_broadcast([P, J, P]),
                                  rel[:, b, :].unsqueeze(2).to_broadcast([P, J, P]), ALU.is_equal).then_inc(s_oh, 1)

            def scan(s, b):
                dve.wait_ge(s_ast, s + 1)
                dve.wait_ge(s_pent, s + 1)
                dve.tensor_tensor_scan(scan_s[:, b, :], pen_t[:, b, :], ps[0:J * HEADS, 4 + b, 0:P], -BIG,
                                       ALU.add, ALU.max).then_inc(s_scan, 1)

            def tile_maxima(s, b):
                g = load(grp_i, s, GROUPS - 1)
                last = lasts[:, bass.ds(g * J, J)].unsqueeze(2)
                dve.wait_ge(s_back, s + 1)
                dve.tensor_tensor(mt[:, b, :, 0:HEADS], ps[:, 4 + b, 256:320].rearrange("p (j h) -> p j h", j=J),
                                  last.to_broadcast([P, J, HEADS]), ALU.mult).then_inc(s_mt, 1)
                dve.tensor_scalar(mt[:, b, :, HEADS:], last, 1.0, None, ALU.mult).then_inc(s_mt, 1)

            def new_maxima(s, b):
                w = load(win_i, s, W - 1)

                def link(n, ins):
                    ins.then_inc(s_ch, 1)
                    dve.wait_ge(s_ch, CH * s + n)
                pm = ps[:, 4 + b, 384:384 + 9 * J].rearrange("p (j c) -> p j c", j=J)
                r_w = run_max[:, bass.ds(w, 1), :]
                old = shift[:, bass.ds(w, 1), :]
                dve.wait_ge(s_pm, s + 1)
                link(1, dve.tensor_scalar(absent[:].unsqueeze(2), pm[:, :, HEADS:], BIG, -BIG, ALU.mult, ALU.add))
                link(2, dve.tensor_tensor(cand, pm[:, :, 0:HEADS], absent[:].unsqueeze(2).to_broadcast([P, J, HEADS]), ALU.add))
                link(3, dve.tensor_reduce(gmax[:], cand.rearrange("p j h -> p h j"), AX.X, ALU.max))
                link(4, dve.tensor_tensor(r_w, r_w, gmax[:].unsqueeze(1), ALU.max))
                link(5, dve.tensor_tensor(zc[:].unsqueeze(1), r_w, a_dst[:, bass.ds(w, 1), :], ALU.add))
                dve.tensor_scalar(adc[:, b, 0:HEADS].unsqueeze(1), a_dst[:, bass.ds(w, 1), :], 1.0, None, ALU.mult).then_inc(s_ch, 1)
                link(7, dve.scalar_tensor_tensor(adc[:, b, HEADS:], zc[:], SLOPE, zc[:], ALU.mult, ALU.max))
                if not isinstance(s, int):
                    dve.wait_ge(s_fac, s - 1)
                link(8, dve.tensor_tensor(grew[:, b, :].unsqueeze(1), old, adc[:, b, HEADS:].unsqueeze(1), ALU.subtract))
                link(9, dve.tensor_scalar(old, adc[:, b, HEADS:].unsqueeze(1), 1.0, None, ALU.mult))

            def scores(s, b):
                e = ps[:, 6, 128 * b:128 * b + 128].rearrange("p (j c) -> p j c", j=J)
                sc = score[:, b, :].rearrange("p (j h) -> p j h", j=J)

                def link(n, ins):
                    ins.then_inc(s_sc, 1)
                    dve.wait_ge(s_sc, 8 + 4 * s + n)
                dve.wait_ge(s_ade, s + 1)
                dve.wait_ge(s_as, s + 1)
                link(1, dve.tensor_tensor(sc, as_s[:, b, :].rearrange("p (j h) -> p j h", j=J), e[:, :, 0:HEADS], ALU.add))
                link(2, dve.scalar_tensor_tensor(sc, sc, SLOPE, sc, ALU.mult, ALU.max))
                link(3, dve.tensor_tensor(sc, sc, e[:, :, HEADS:], ALU.subtract))
                dve.tensor_scalar(sc, sc, 1.0, None, ALU.min).then_inc(s_sc, 1)

            def message(s, b, q, slot):
                if q == 0:
                    dve.wait_ge(s_w, s + 1)
                    if not isinstance(s, int):
                        dve.wait_ge(s_seg, s - 1)
                jj = slice(2 * q, 2 * q + 2)
                weight = weights[:, b, 16 * q:16 * q + 16].rearrange("p (j h) -> p j h", h=HEADS)
                dve.tensor_tensor(msg[:, b, jj, :].rearrange("p j (h c) -> p j h c", c=HC),
                                  ring[:, bass.ds(slot, 1), jj, 0:ROW].rearrange("p s j (h c) -> p (s j) h c", c=HC),
                                  weight.unsqueeze(3).to_broadcast([P, 2, HEADS, HC]),
                                  ALU.mult).then_inc(s_msg, 1)

            def add_sums(s, b):
                w = load(win_i, s, W - 1)
                acc = nodes[:, bass.ds(w, 1), :].rearrange("p w c -> p (w c)")
                dve.wait_ge(s_fac, s + 1)
                dve.wait_ge(s_acc, 4 + 2 * s)
                dve.tensor_tensor(rescaled.rearrange("p (h c) -> p h c", c=HC), acc.rearrange("p (h c) -> p h c", c=HC),
                                  factor[:, b, :].unsqueeze(2).to_broadcast([P, HEADS, HC]), ALU.mult).then_inc(s_acc, 1)
                dve.wait_ge(s_acc, 4 + 2 * s + 1)
                dve.wait_ge(s_seg, s + 1)
                dve.tensor_tensor(acc, rescaled, ps[:, 2 + b, 0:ROW], ALU.add).then_inc(s_acc, 1)
            for s in range(2):
                make_onehot(s, s)
            scan(0, 0)
            tile_maxima(0, 0)
            new_maxima(0, 0)
            scores(0, 0)

            def step(s, b, before=True, nxt=True, after=True):
                slot = load(grp_i, s, GROUPS - 1) % RING
                if nxt:
                    scan(s + 1, 1 - b)
                message(s, b, 0, slot)
                if nxt:
                    tile_maxima(s + 1, 1 - b)
                message(s, b, 1, slot)
                if before:
                    add_sums(s - 1, 1 - b)
                if nxt:
                    new_maxima(s + 1, 1 - b)
                message(s, b, 2, slot)
                if nxt:
                    scores(s + 1, 1 - b)
                message(s, b, 3, slot)
                if after:
                    dve.wait_ge(s_seg, s + 1)
                    make_onehot(s + 2, b)
            step(0, 0, before=False)
            step(1, 1)
            with dve.Fori(2, STEPS - 3, 2) as t:
                for b in range(2):
                    step(t + b, b)
            step(STEPS - 2, 0, after=False)
            step(STEPS - 1, 1, nxt=False, after=False)
            add_sums(STEPS - 1, 1)

            dve.sem_inc(s_r, 1)
            with dve.Fori(0, CHUNKS) as i:
                part = nodes[:, bass.ds(i * CW, CW), :].rearrange("p w (h c) -> p (w h) c", c=HC)

                def link(n, ins):
                    ins.then_inc(s_r, 1)
                    dve.wait_ge(s_r, 1 + i * RS + n)
                iv = inv[:].rearrange("p w h -> p (w h)").unsqueeze(2)
                link(1, dve.tensor_scalar(iv, part[:, :, HD:HC], DEN_EPS, None, ALU.add))
                link(2, dve.reciprocal(iv, iv))
                link(3, dve.tensor_tensor(gat.rearrange("p w (h c) -> p (w h) c", c=HD), part[:, :, 0:HD],
                                          iv.to_broadcast([P, CW * HEADS, HD]), ALU.mult))
                link(4, dve.tensor_tensor(gat, gat, bias[:].unsqueeze(1).to_broadcast([P, CW, D]), ALU.add))
                dve.wait_ge(s_xa, i * 16 + 16)
                link(5, dve.scalar_tensor_tensor(gat, gat, 0.0, x_again, ALU.max, ALU.add))
                dve.wait_ge(s_mix, CW + i * CW + CW)
                x1 = nodes[:, bass.ds(i * CW, CW), 0:D]
                link(6, dve.tensor_tensor(x1, gat, ps[:, 0:4, :].rearrange("p b n -> p (b n)")[:, 0:CW * D]
                                          .rearrange("p (w c) -> p w c", c=D), ALU.add))
                settle(dve)
                for k in range(CW):
                    dve.bn_stats(stats[:, k, :], nodes[:, bass.ds(i * CW + k, 1), 0:D].rearrange("p w c -> p (w c)")).then_inc(s_r, 1)
                dve.wait_ge(s_r, i * RS + 7 + CW)
                settle(dve)
                for k in range(CW):
                    dve.bn_aggr(mv[:, k, :], stats[:, k, :]).then_inc(s_r, 1)
                dve.wait_ge(s_r, i * RS + 7 + 2 * CW)
                link(RS, dve.tensor_scalar(mv2[:, bass.ds(i * CW, CW), :], mv[:], 1.0, None, ALU.mult))
            dve.wait_ge(s_sd2, 1)
            dve.reciprocal(rstd2[:], rstd2[:]).then_inc(s_rs2, 1)
            dve.wait_ge(s_rs2, 1)
            dve.sem_inc(s_y, 3)
            with dve.Fori(0, CHUNKS) as c:
                for k in range(CW):
                    w = c * CW + k
                    dve.tensor_scalar(xn2[:, k, :].unsqueeze(1), nodes[:, bass.ds(w, 1), 0:D],
                                      mv2[:, bass.ds(w, 1), 0:1].rearrange("p w c -> p (w c)"), rstd2[:, bass.ds(w, 1)],
                                      ALU.subtract, ALU.mult).then_inc(s_n2, 1)

                def link(n, ins):
                    ins.then_inc(s_g, 1)
                    dve.wait_ge(s_g, c * 5 + n)
                dve.wait_ge(s_lg, c + 1)
                logits = ps[:, 7, 0:CW * EXPERTS].rearrange("p (k e) -> p k e", e=EXPERTS)
                link(1, dve.tensor_reduce(lmax[:], logits, AX.X, ALU.max))
                link(2, dve.tensor_tensor(lg[:], logits, lmax[:].unsqueeze(2).to_broadcast([P, CW, EXPERTS]), ALU.subtract))
                dve.wait_ge(s_ge, c + 1)
                link(3, dve.tensor_reduce(lsum[:], lg[:], AX.X, ALU.add))
                link(4, dve.reciprocal(lsum[:], lsum[:]))
                link(5, dve.tensor_tensor(gate[:], lg[:], lsum[:].unsqueeze(2).to_broadcast([P, CW, EXPERTS]), ALU.mult))
                dve.wait_ge(s_yfree, c + 1)
                for k in range(CW):
                    dve.wait_ge(s_l3, c * YT + (k + 1))
                    dve.tensor_tensor(y[:, k, :].unsqueeze(1), ps[:, 4 + k % 3, 0:D].unsqueeze(1),
                                      nodes[:, bass.ds(c * CW + k, 1), 0:D], ALU.add).then_inc(s_y, 1)
                for e in range(EXPERTS):
                    for k in range(CW):
                        n = CW * (e + 1) + k
                        dve.wait_ge(s_l3, c * YT + (n + 1))
                        dve.wait_ge(s_y, 3 + c * YT + (n + 1 - CW))
                        dve.scalar_tensor_tensor(y[:, k, :], ps[:, 4 + n % 3, 0:D], gate[:, k, e:e + 1], y[:, k, :],
                                                 ALU.mult, ALU.add).then_inc(s_y, 1)


STEP_TABLES = 6
SETUP_DONE = STEP_TABLES + 3 + 5 + 1 + 8 + 2 + 5 + 2
CTX_DONE = 5 + 3 + 4 + 2


def kernel(**inputs):
    import numpy as np
    import concourse.bacc as bacc
    from concourse.bass_utils import run_bass_kernel_spmd as run

    nc = bacc.Bacc("TRN2", target_bir_lowering=False, num_devices=1)
    arrays = {}
    a = {k: np.asarray(v) for k, v in inputs.items()}

    def give(name, array):
        arrays[name] = np.ascontiguousarray(array)
        return nc.dram_tensor(name, arrays[name].shape, mybir.dt.from_np(arrays[name].dtype), kind="ExternalInput").ap()

    x = np.zeros((W * P, D), np.float32)
    x[:NODES] = a["x"]
    slots = GROUPS * GROUP
    src = np.zeros(slots, np.int32)
    src[:EDGES] = a["src"]
    dst = np.full(slots, W * P, np.int32)
    dst[:EDGES] = a["dst"]
    before = np.concatenate([[-1], dst[:-1]]).astype(np.int32)
    after = np.concatenate([dst[1:], [-1]]).astype(np.int32)
    after[P - 1::P] = -1
    by_edge = np.stack([v.reshape(GROUPS * J, P).T for v in (dst, before, after)], 1)
    w_h = np.zeros((D, PROJ), np.float32)
    w_h[:, :ROW].reshape(D, HEADS, HC)[:, :, :HD] = a["L0_gnn_W"]
    qkv = a["L0_mix_W_qkv"]
    proj = np.concatenate([w_h, qkv[:, MD:3 * MD], qkv[:, :MD]], 1).reshape(2, P, -1).transpose(1, 0, 2)
    rows = np.concatenate([a["L0_gnn_att_src"].ravel(), a["L0_gnn_att_dst"].ravel(), a["L0_gnn_bias"], a["L0_mix_b_out"]])
    ffn = np.stack([a[f"L0_ffn_{n}"].reshape(EXPERTS, 2, P, D).transpose(2, 0, 1, 3) for n in ("W1", "W2", "Wo")], 1)
    bn = np.stack([np.stack([a[f"L0_ffn_{n}{l}"].reshape(2 * EXPERTS, P).T for l in (1, 2)], 1)
                   for n in ("b", "g", "be", "m", "v")], 1)
    args = [
        give("x", x), give("src", src.reshape(GROUPS, J, P).transpose(0, 2, 1)), give("dst", by_edge),
        give("dst_last", dst.reshape(GROUPS, GROUP)[:, -1][None]), give("rows", rows[None]), give("wproj", proj),
        give("wout", a["L0_mix_W_out"]), give("wffn", ffn.reshape(P, -1)), give("bn", bn),
        give("wr", a["L0_ffn_Wr"].reshape(2, P, EXPERTS).transpose(1, 0, 2)), give("br", a["L0_ffn_br"][None]),
        give("bo", a["L0_ffn_bo"]),
        nc.dram_tensor("table", (W * P, TROW), F32, kind="Internal").ap(),
        nc.dram_tensor("out", (W * P, D), F32, kind="ExternalOutput").ap(),
    ]
    gps_layer(nc, *args)
    r = run(nc, [arrays], core_ids=[0])
    return r.results[0]["out"][:NODES]
```
